# Optimizing a Trainium2 kernel written in Bass

```python
import numpy as np
import jax
import jax.numpy as jnp

def _softmax(x, axis=-1):
    return jax.nn.softmax(x, axis=axis)

def _gelu(x):
    return jax.nn.gelu(x, approximate=True)

def _silu(x):
    return jax.nn.silu(x)

def _sigmoid(x):
    return jax.nn.sigmoid(x)

def _layernorm(x, axis=-1, eps=1e-05):
    m = jnp.mean(x, axis=axis, keepdims=True)
    v = jnp.var(x, axis=axis, keepdims=True)
    return (x - m) / jnp.sqrt(v + eps)

def _scatter_add(tgt, idx, src, axis=0):
    return tgt.at[idx].add(src)

def _segment_sum(src, seg, n):
    return jax.ops.segment_sum(src, seg, n)
kernel_name = 'mk_adj_preln_d1_adj_r2_eeea70'

def setup_inputs(seed: int=0):
    np.random.seed(seed)
    _w = jnp.asarray

    def _rec_inputs():
        import jax
        import jax.numpy as jnp
        _gk = jax.random.key(seed)
        x = -0.0005207 + 1.001 * jax.random.normal(jax.random.fold_in(_gk, 1), (4096, 128), jnp.float32)
        _a = jax.random.bernoulli(jax.random.fold_in(_gk, 2), 0.00195312, (4096, 4096))
        adj = _a.astype(jnp.int32)
        return (x, adj)
    x, adj = _rec_inputs()

    def _L0_gnn_setup():
        import jax, jax.numpy as jnp
        import numpy as np
        ALPHA = 0.2
        MASK_VAL = -9000000000000000.0
        key = jax.random.key(seed)
        k1, k2, k3, k4 = jax.random.split(key, 4)
        N, Fin, Fout = (4096, 128, 128)
        h = jax.random.normal(k1, (N, Fin), dtype=jnp.float32)
        adj = jax.random.randint(k2, (N, N), 0, 2, dtype=jnp.int32)
        W = jax.random.normal(k3, (Fin, Fout), dtype=jnp.float32) * 0.06
        a = jax.random.normal(k4, (2 * Fout, 1), dtype=jnp.float32) * 0.06
        return {'h': h, 'adj': adj, 'W': W, 'a': a}
    _L0_gnn_all = _L0_gnn_setup()
    _L0_gnn_in = {k: v for k, v in _L0_gnn_all.items() if k in ('W', 'a')}
    del _L0_gnn_all
    return {'x': x, 'adj': adj, 'L0_gnn_W': _L0_gnn_in['W'], 'L0_gnn_a': _L0_gnn_in['a']}

def reference(x, adj, L0_gnn_W, L0_gnn_a):
    import jax
    import jax.numpy as jnp

    def _L0_gnn_ref(h, adj, W, a):
        import jax, jax.numpy as jnp
        import numpy as np
        ALPHA = 0.2
        MASK_VAL = -9000000000000000.0
        Fout = W.shape[1]
        Wh = h @ W
        a1, a2 = (a[:Fout, 0], a[Fout:, 0])
        e = (Wh @ a1)[:, None] + (Wh @ a2)[None, :]
        e = jnp.where(e > 0, e, ALPHA * e)
        e = jnp.where(adj > 0, e, MASK_VAL)
        attention = jax.nn.softmax(e, axis=1)
        h_prime = attention @ Wh
        return jax.nn.elu(h_prime)
    h = jnp.maximum(_layernorm(x, axis=-1), 0.0)
    x = x + _L0_gnn_ref(h, adj, L0_gnn_W, L0_gnn_a)
    return x

_drawn_inputs = setup_inputs


def setup_inputs(seed=0):
    import zlib

    import numpy as np

    out = dict(_drawn_inputs(seed))
    spreads = {}
    factors = {}
    for name, (base, spread) in spreads.items():
        noise = np.random.default_rng([zlib.crc32(name.encode()), seed]).standard_normal(out[name].shape)
        drawn = base * np.exp(spread * noise) if base else spread * noise
        out[name] = jnp.asarray(drawn.astype(out[name].dtype))
    for name, factor in factors.items():
        out[name] = (out[name] * factor).astype(out[name].dtype)
    return out
```

```python
from contextlib import ExitStack
import math

import concourse.bass as bass
from concourse import mybir

ALU = mybir.AluOpType
ACT = mybir.ActivationFunctionType
AX = mybir.AxisListType
F32 = mybir.dt.float32
F16 = mybir.dt.float16
BF16 = mybir.dt.bfloat16
I32 = mybir.dt.int32
U32 = mybir.dt.uint32
U8 = mybir.dt.uint8

P = 128
Q4 = 4
GROUP = Q4 * P
EPS = 1e-5
ALPHA = 0.2

B = 1.0 - ALPHA
LOG_WEIGHT = 7.5 * math.log(2.0)
LOG_VALUE = 10.0 * math.log(2.0)
SEED = 2.0 ** -60

RING = 4
POOL_TILES = 2


def bass_graph_attention(nc: bass.Bass, x: bass.AP, adj: bass.AP, w: bass.AP, a: bass.AP, out: bass.AP):
    N, F = x.shape
    T = N // P
    G = N // GROUP
    CT = 8
    CHUNK = CT * P
    C = N // CHUNK
    H = G // RING
    STEPS = T // CT
    V = F + 1
    VP = V + 3
    LO, HI = 0, 1
    assert F == P and w.shape == (F, F) and T % CT == 0 and G % RING == 0 and STEPS >= 2

    x_v = x.rearrange("(g p q) f -> p g q f", p=P, q=Q4)
    out_v = out.rearrange("(g p q) f -> g p q f", p=P, q=Q4)
    adj_v = adj.rearrange("(r p q) (g j) -> g r p q j", p=P, q=Q4, j=GROUP)

    with ExitStack() as ctx:
        def sb(name, shape, dt):
            return ctx.enter_context(nc.sbuf_tensor(name, shape, dt))

        def ps(name, shape, dt):
            return ctx.enter_context(nc.psum_tensor(name, shape, dt))

        def sem(name):
            return ctx.enter_context(nc.semaphore(name))

        x_sb = sb("x_sb", [P, T, F], F32)
        raw = sb("raw", [P, RING, CT, GROUP], I32)
        mask = sb("mask", [P, RING, CT, GROUP], U8)
        words = sb("words", [P, RING, CHUNK], F32)
        g_row = sb("g_row", [P, N], F32)
        val = sb("val", [P, T, 2, VP], F16)
        h_t = sb("h_t", [P, N], F32)
        hn = sb("hn", [P, 2, CT, F], F32)
        v32 = sb("v32", [P, 2, CT, F], F32)
        w_sb = sb("w_sb", [P, F], F32)
        a_row = sb("a_row", [P, 2, F], F32)
        wa_prod = sb("wa_prod", [P, 2, F], F32)
        wa = sb("wa", [P, 2], F32)
        ident = sb("ident", [P, P], F32)
        ident_b = sb("ident_b", [P, P], BF16)
        seed_w = sb("seed_w", [P, P], BF16)
        log_weight = sb("log_weight", [P, 1], F32)
        log_value = sb("log_value", [P, 1], F32)
        step_bias = sb("step_bias", [P, 1], F32)
        minus_half = sb("minus_half", [P, CT], F32)
        stats = sb("stats", [P, T, 6], F32)
        mv = sb("mv", [P, T, 2], F32)
        var_eps = sb("var_eps", [P, T], F32)
        rstd = sb("rstd", [P, T], F32)
        nmr = sb("nmr", [P, T], F32)
        gq = sb("gq", [P, 2, T], F32)
        gq_hi = sb("gq_hi", [P, 2, T], F32)
        gq_word = sb("gq_word", [P, 2, T], F32)
        dv = sb("dv", [P, T], F32)
        h_sums = sb("h_sums", [P, 2 * STEPS], F32)
        h_sum = sb("h_sum", [P, 1], F32)
        mean32 = sb("mean32", [P, 3, V], F32)
        mean_hl = sb("mean_hl", [P, 2, 3, V], F16)
        acc_sb = sb("acc_sb", [P, 3, 3, V], F32)
        rz = sb("rz", [P, 3, 3], F32)
        hp = sb("hp", [P, CT, F], F32)
        neg = sb("neg", [P, CT, F], F32)
        pos = sb("pos", [P, CT, F], F32)
        res = sb("res", [P, CT, F], F32)

        acc = ps("acc", [P, 3, 512], F32)
        mask_t = ps("mask_t", [P, 2, 2, 512], F32)
        f_ps = ps("f_ps", [P, 512], F32)

        words_h = words[:].bitcast(F16).rearrange("p s (i e) -> p s i e", e=2)
        gq_word_h = gq_word[:].bitcast(F16).rearrange("p u (t e) -> p u t e", e=2)
        mask_pairs = mask[:].bitcast(BF16).rearrange("p s t (j h) -> p s t j h", h=2)
        maskt_pairs = mask_t[:].bitcast(BF16)
        maskt_bytes = mask_t[:].bitcast(U8).rearrange("p s h (i e) -> p s h i e", e=2)

        def acc_of(t):
            return acc[:, t // 3, (t % 3) * V:(t % 3 + 1) * V]

        x_in = [sem(f"x_in{k}") for k in range(STEPS)]
        w_in = sem("w_in")
        raw_in = [sem(f"raw_in{s}") for s in range(RING)]
        pool_bytes = sem("pool_bytes")
        act_bytes = sem("act_bytes")
        turned = sem("turned")
        words_ready = sem("words_ready")
        words_free = sem("words_free")
        acc_free = sem("acc_free")
        ident_ready = sem("ident_ready")
        consts = sem("consts")
        dve_chain = sem("dve_chain")
        var_ready = sem("var_ready")
        rstd_ready = sem("rstd_ready")
        hn_ready = sem("hn_ready")
        wa_ready = sem("wa_ready")
        ht_ps = sem("ht_ps")
        ht_ready = sem("ht_ready")
        f_ready = sem("f_ready")
        wh_ps = sem("wh_ps")
        exps_ready = sem("exps_ready")
        word_ready = sem("word_ready")
        v32_ready = sem("v32_ready")
        vh_ready = sem("vh_ready")
        vl_ready = sem("vl_ready")
        z_ready = sem("z_ready")
        grow_ps = sem("grow_ps")
        grow_ready = sem("grow_ready")
        hsum_ready = sem("hsum_ready")
        mean_ps = sem("mean_ps")
        mean_ready = sem("mean_ready")
        rz_ready = sem("rz_ready")
        hp_ready = sem("hp_ready")
        neg_ready = sem("neg_ready")
        pos_ready = sem("pos_ready")
        ex_ready = sem("ex_ready")
        sum_ready = sem("sum_ready")
        res_ready = sem("res_ready")
        out_done = sem("out_done")

        block = ctx.enter_context(nc.Block())

        @block.sync
        def _(sp):
            for k in range(STEPS):
                sp.dma_start(x_sb[:, k * CT:(k + 1) * CT, :].rearrange("p (g q) f -> p g q f", q=Q4),
                             x_v[:, 2 * k:2 * k + 2]).then_inc(x_in[k], 16)
                if k == 0:
                    sp.dma_start(w_sb[:], w).then_inc(w_in, 16)
                    sp.dma_start(a_row[:], a.rearrange("(k f) o -> o k f", k=2).broadcast_to([P, 2, F])).then_inc(w_in, 16)

            def load(c, g, s):
                for r in range(2):
                    sp.dma_start(raw[:, s, r * Q4:(r + 1) * Q4],
                                 adj_v[bass.ds(g, 1), bass.ds(c * 2 + r, 1)].rearrange("o r p q j -> (o r p) q j")
                                 ).then_inc(raw_in[s], 16)

            with sp.Fori(0, C) as c:
                with sp.Fori(0, H) as h:
                    for s in range(RING):
                        sp.wait_ge(pool_bytes, (c * H + h) * RING + s + 1)
                        sp.wait_ge(act_bytes, (c * H + h) * RING + s + 1)
                        load(c, h * RING + s, s)
            sp.wait_ge(out_done, 16 * 2 * C)

        @block.gpsimd
        def _(pool):
            nc.gpsimd.memset(ident[:], 0.0).then_inc(ident_ready, 1)
            pool.wait_ge(ident_ready, 1)
            nc.gpsimd.affine_select(out=ident[:], in_=ident[:], compare_op=ALU.not_equal, fill=1.0, base=0,
                                    pattern=[[-1, P]], channel_multiplier=1).then_inc(ident_ready, 1)
            pool.wait_ge(ident_ready, 2)
            nc.gpsimd.tensor_copy(ident_b[:], ident[:]).then_inc(ident_ready, 1)
            nc.gpsimd.memset(seed_w[:], SEED / P).then_inc(consts, 1)
            pool.sem_inc(pool_bytes, RING)
            pool.sem_inc(act_bytes, RING)
            pool.sem_inc(hp_ready, 1)
            for k in range(STEPS):
                t0 = k * CT
                pool.wait_ge(var_ready, k + 1)
                nc.gpsimd.tensor_tensor(rstd[:, t0:t0 + CT], var_eps[:, t0:t0 + CT], minus_half[:], ALU.pow).then_inc(rstd_ready, 1)
            for k in range(STEPS):
                t0 = k * CT
                pool.wait_ge(vh_ready, k + 1)
                nc.gpsimd.tensor_tensor(val[:, t0:t0 + CT, 0 + 1, 0:F], v32[:, k % 2], val[:, t0:t0 + CT, 0, 0:F],
                                        ALU.subtract).then_inc(vl_ready, 1)

            def to_bytes(c, h):
                for s in range(RING):
                    pool.wait_ge(raw_in[s], (c * H + h + 1) * 32)
                    pool.wait_ge(turned, (c * H + h) * RING + s + 1)
                    pool.nop(nofuse=True)
                    nc.gpsimd.tensor_scalar(mask[:, s, 0:POOL_TILES], raw[:, s, 0:POOL_TILES], 0, None,
                                            ALU.is_gt).then_inc(pool_bytes, 1)

            def tail(c):
                pool.wait_ge(rz_ready, c + 1)
                for b in range(3):
                    n = min(3, CT - 3 * b)
                    last = nc.gpsimd.tensor_tensor(hp[:, 3 * b:3 * b + n], acc_sb[:, b, 0:n, 0:F],
                                                   rz[:, b, 0:n].unsqueeze(2).broadcast_to([P, n, F]), ALU.mult)
                last.then_inc(hp_ready, 1)
                pool.wait_ge(hp_ready, c + 2)
                pool.nop(nofuse=True)
                nc.gpsimd.tensor_scalar(neg[:], hp[:], 0.0, None, ALU.min).then_inc(neg_ready, 1)
                pool.wait_ge(pos_ready, c + 1)
                nc.gpsimd.tensor_tensor(pos[:], pos[:], x_sb[:, bass.ds(c * CT, CT)], ALU.add).then_inc(sum_ready, 1)

            with pool.Fori(0, H) as h:
                to_bytes(0, h)
            with pool.Fori(1, C) as c:
                to_bytes(c, 0)
                tail(c - 1)
                for h in range(1, H):
                    to_bytes(c, h)
            pool.drain().then_inc(pool_bytes, 1)
            tail(C - 1)

        @block.scalar
        def _(act):
            act.sem_inc(acc_free, 3)
            act.wait_ge(consts, 4)
            for k in range(STEPS):
                t0 = k * CT
                for b in range(2):
                    act.wait_ge(ht_ps, 2 * k + b + 1)
                    nc.scalar.activation(h_t[:, t0 * P + b * 512:t0 * P + (b + 1) * 512], mask_t[:, k % 2, b, :], ACT.Relu,
                                         accum_out=h_sums[:, 2 * k + b:2 * k + b + 1]).then_inc(ht_ready, 1)
                act.wait_ge(f_ready, k + 1)
                f1, f2 = (f_ps[:, 0:2 * CT].rearrange("p (t u) -> p t u", u=2)[:, :, u] for u in range(2))
                nc.scalar.activation(gq[:, 0, t0:t0 + CT], f1, ACT.Exp, scale=-B, bias=log_weight[:, 0:1]).then_inc(exps_ready, 1)
                nc.scalar.activation(gq[:, 1, t0:t0 + CT], f2, ACT.Exp, scale=B, bias=log_weight[:, 0:1]).then_inc(exps_ready, 1)
                nc.scalar.activation(dv[:, t0:t0 + CT], f2, ACT.Exp, scale=ALPHA, bias=log_value[:, 0:1]).then_inc(exps_ready, 1)
                for b in range(2):
                    act.wait_ge(grow_ps, 2 * k + b + 1)
                    nc.scalar.copy(g_row[:, t0 * P + b * 512:t0 * P + (b + 1) * 512], mask_t[:, k % 2, b, :]).then_inc(grow_ready, 1)
                act.wait_ge(v32_ready, 2 * k + 2)
                nc.scalar.copy(val[:, t0:t0 + CT, 0, 0:F], v32[:, k % 2]).then_inc(vh_ready, 1)

            def to_bytes(c, h):
                for s in range(RING):
                    act.wait_ge(raw_in[s], (c * H + h + 1) * 32)
                    act.wait_ge(turned, (c * H + h) * RING + s + 1)
                    nc.scalar.activation(mask[:, s, POOL_TILES:CT], raw[:, s, POOL_TILES:CT], ACT.Sigmoid, scale=64.0,
                                         bias=step_bias[:, 0:1]).then_inc(act_bytes, 1)

            def tail(c):
                act.wait_ge(words_free, RING + (c + 1) * G * Q4)
                act.wait_ge(hp_ready, c + 1)
                for b in range(3):
                    nc.scalar.copy(acc_sb[:, b], acc[:, b, 0:3 * V].rearrange("p (t v) -> p t v", v=V)).then_inc(acc_free, 1)
                act.wait_ge(hp_ready, c + 2)
                nc.scalar.activation(pos[:], hp[:], ACT.Relu).then_inc(pos_ready, 1)
                act.wait_ge(neg_ready, c + 1)
                nc.scalar.activation(neg[:], neg[:], ACT.Exp).then_inc(ex_ready, 1)

            def store(c):
                act.wait_ge(res_ready, c + 1)
                for r in range(2):
                    act.dma_start(out_v[bass.ds(2 * c + r, 1)].rearrange("o p q f -> (o p) q f"),
                                  res[:, r * Q4:(r + 1) * Q4]).then_inc(out_done, 16)

            with act.Fori(0, H) as h:
                to_bytes(0, h)
            with act.Fori(1, C) as c:
                to_bytes(c, 0)
                tail(c - 1)
                store(c - 1)
                for h in range(1, H):
                    to_bytes(c, h)
                act.wait_ge(out_done, 32 * c)
            act.drain().then_inc(act_bytes, 1)
            tail(C - 1)
            store(C - 1)

        @block.vector
        def _(dve):
            links = [0]

            def link(ins):
                links[0] += 1
                ins.then_inc(dve_chain, 1)
                dve.wait_ge(dve_chain, links[0])

            dve.sem_inc(words_ready, Q4)
            nc.vector.memset(log_weight[:], LOG_WEIGHT).then_inc(consts, 1)
            nc.vector.memset(log_value[:], LOG_VALUE).then_inc(consts, 1)
            nc.vector.memset(step_bias[:], -32.0).then_inc(consts, 1)
            link(nc.vector.memset(minus_half[:], -0.5))

            def moments(k):
                dve.wait_ge(x_in[k], 16)
                for t in range(k * CT, (k + 1) * CT):
                    last = nc.vector.bn_stats(stats[:, t, :], x_sb[:, t, :])
                link(last)
                for t in range(k * CT, (k + 1) * CT):
                    last = nc.vector.bn_aggr(mv[:, t, :], stats[:, t, :])
                link(last)
                nc.vector.tensor_scalar(var_eps[:, k * CT:(k + 1) * CT], mv[:, k * CT:(k + 1) * CT, 1], EPS, None,
                                        ALU.add).then_inc(var_ready, 1)

            def normalise(k):
                dve.wait_ge(rstd_ready, k + 1)
                tt = slice(k * CT, (k + 1) * CT)
                link(nc.vector.scalar_tensor_tensor(nmr[:, tt], mv[:, tt, 0], -1.0, rstd[:, tt], ALU.mult, ALU.mult))
                if k >= 2:
                    dve.wait_ge(ht_ps, 2 * k - 2)
                for i in range(CT):
                    t = k * CT + i
                    last = nc.vector.tensor_scalar(hn[:, k % 2, i], x_sb[:, t], rstd[:, t:t + 1], nmr[:, t:t + 1],
                                                   ALU.mult, ALU.add)
                last.then_inc(hn_ready, 1)

            def make_words(k):
                tt = slice(k * CT, (k + 1) * CT)
                dve.wait_ge(exps_ready, 3 * k + 3)
                link(nc.vector.tensor_scalar(gq_hi[:, :, tt].bitcast(U32), gq[:, :, tt].bitcast(U32), 0xFFFFE000, None,
                                             ALU.bitwise_and))
                nc.vector.tensor_copy(gq_word_h[:, :, tt, HI], gq_hi[:, :, tt]).then_inc(word_ready, 1)
                nc.vector.tensor_tensor(gq_word_h[:, :, tt, LO], gq[:, :, tt], gq_hi[:, :, tt], ALU.subtract).then_inc(word_ready, 1)
                link(nc.vector.tensor_copy(val[:, tt, 0, F], dv[:, tt]))
                nc.vector.tensor_tensor(val[:, tt, 1, F], dv[:, tt], val[:, tt, 0, F], ALU.subtract).then_inc(z_ready, 1)

            def weigh(k):
                if k >= 2:
                    dve.wait_ge(vl_ready, k - 1)
                for b in range(2):
                    dve.wait_ge(wh_ps, 2 * k + b + 1)
                    t0 = k * CT + b * Q4
                    nc.vector.tensor_tensor(v32[:, k % 2, b * Q4:(b + 1) * Q4], acc[:, b, :].rearrange("p (t f) -> p t f", f=F),
                                            dv[:, t0:t0 + Q4].unsqueeze(2).broadcast_to([P, Q4, F]), ALU.mult
                                            ).then_inc(v32_ready, 1)

            moments(0)
            dve.wait_ge(w_in, 32)
            link(nc.vector.tensor_tensor(wa_prod[:], a_row[:], w_sb[:].unsqueeze(1).broadcast_to([P, 2, F]), ALU.mult))
            nc.vector.tensor_reduce(wa[:], wa_prod[:], AX.X, ALU.add).then_inc(wa_ready, 1)
            normalise(0)
            for k in range(STEPS):
                if k + 1 < STEPS:
                    moments(k + 1)
                    normalise(k + 1)
                make_words(k)
                weigh(k)
            dve.wait_ge(ht_ready, 2 * STEPS)
            nc.vector.tensor_reduce(h_sum[:], h_sums[:], AX.X, ALU.add).then_inc(hsum_ready, 1)
            dve.wait_ge(mean_ps, 1)
            link(nc.vector.memset(mean32[:], 2.0 ** 10))
            for b in range(3):
                last = nc.vector.tensor_scalar(mean32[:, b, 0:F], f_ps[:, 128:128 + F], 2.0 ** 10 / N, None, ALU.mult)
            link(last)
            link(nc.vector.tensor_copy(mean_hl[:, 0], mean32[:]))
            nc.vector.tensor_tensor(mean_hl[:, 1], mean32[:], mean_hl[:, 0], ALU.subtract).then_inc(mean_ready, 1)

            dve.wait_ge(grow_ready, 2 * STEPS)

            def weights(c, h, s):
                for q in range(Q4):
                    u = (c * H + h) * RING + s
                    if q == 0:
                        dve.wait_ge(turned, RING + u + 1)
                    dve.wait_ge(words_free, u * Q4 + q + 1)
                    nc.vector.scalar_tensor_tensor(words[:, q, :], g_row[:, bass.ds(c * CHUNK, CHUNK)],
                                                   gq_word[:, 1, bass.ds((h * RING + s) * Q4 + q, 1)],
                                                   maskt_bytes[:, s % 2, q // 2, :, q % 2], ALU.max, ALU.mult).then_inc(words_ready, 1)

            def reciprocals(c):
                dve.wait_ge(acc_free, 3 * (c + 2))
                nc.vector.reciprocal(rz[:], acc_sb[:, :, :, F]).then_inc(rz_ready, 1)

            def result(c):
                dve.wait_ge(ex_ready, c + 1)
                dve.wait_ge(sum_ready, c + 1)
                nc.vector.scalar_tensor_tensor(res[:], neg[:], -1.0, pos[:], ALU.add, ALU.add).then_inc(res_ready, 1)

            with dve.Fori(0, H) as h:
                for s in range(RING):
                    weights(0, h, s)
            with dve.Fori(1, C) as c:
                weights(c, 0, 0)
                reciprocals(c - 1)
                for s in range(1, RING):
                    weights(c, 0, s)
                result(c - 1)
                for h in range(1, H):
                    for s in range(RING):
                        weights(c, h, s)
            reciprocals(C - 1)
            result(C - 1)

        @block.tensor
        def _(pe):
            pe.sem_inc(turned, RING)
            pe.sem_inc(words_free, RING)
            pe.wait_ge(ident_ready, 3)

            def turn_x(k):
                pe.wait_ge(hn_ready, k + 1)
                if k >= 2:
                    pe.wait_ge(grow_ready, 2 * k - 2)
                for i in range(CT):
                    ins = nc.tensor.transpose(mask_t[:, k % 2, i // Q4, (i % Q4) * P:(i % Q4 + 1) * P], hn[:, k % 2, i], ident[:])
                    if i % Q4 == Q4 - 1:
                        ins.then_inc(ht_ps, 1)

            turn_x(0)
            for k in range(STEPS):
                if k + 1 < STEPS:
                    turn_x(k + 1)
                pe.wait_ge(wa_ready, 1)
                pe.wait_ge(ht_ready, 2 * k + 2)
                if k >= 1:
                    pe.wait_ge(exps_ready, 3 * k)
                for i in range(CT):
                    t = k * CT + i
                    last = nc.tensor.matmul(f_ps[:, 2 * i:2 * i + 2], h_t[:, t * P:(t + 1) * P], wa[:], start=True, stop=True)
                last.then_inc(f_ready, 1)
                for i in range(CT):
                    t = k * CT + i
                    if i % Q4 == 0 and k >= 1:
                        pe.wait_ge(v32_ready, 2 * k - 1 + i // Q4)
                    ins = nc.tensor.matmul(acc[:, i // Q4, (i % Q4) * P:(i % Q4 + 1) * P], h_t[:, t * P:(t + 1) * P], w_sb[:],
                                           start=True, stop=True)
                    if i % Q4 == Q4 - 1:
                        ins.then_inc(wh_ps, 1)
                pe.wait_ge(word_ready, 2 * k + 2)
                for i in range(CT):
                    t = k * CT + i
                    ins = nc.tensor.transpose(mask_t[:, k % 2, i // Q4, (i % Q4) * P:(i % Q4 + 1) * P],
                                              gq_word[:, 0, t:t + 1].broadcast_to([P, P]), ident[:])
                    if i % Q4 == Q4 - 1:
                        ins.then_inc(grow_ps, 1)
            pe.wait_ge(hsum_ready, 1)
            nc.tensor.matmul(f_ps[:, 128:128 + F], h_sum[:, 0:1].broadcast_to([P, P]), w_sb[:], start=True, stop=True).then_inc(mean_ps, 1)

            def turn(u, s):
                pe.wait_ge(pool_bytes, RING + u + 1)
                pe.wait_ge(act_bytes, RING + u + 1)
                for half in range(2):
                    for i in range(CT):
                        last = nc.tensor.transpose(maskt_pairs[:, s % 2, half, i * P:(i + 1) * P], mask_pairs[:, s, i, :, half],
                                                   ident_b[:])
                last.then_inc(turned, 1)

            pe.wait_ge(grow_ready, 2 * STEPS)
            turn(0, 0)
            pe.wait_ge(mean_ready, 1)
            pe.wait_ge(v32_ready, 2 * STEPS)
            pe.wait_ge(vl_ready, STEPS)
            pe.wait_ge(z_ready, STEPS)
            with pe.Fori(0, C) as c:
                for b in range(3):
                    pe.wait_ge(acc_free, 3 * c + b + 1)
                    for e in range(2):
                        nc.tensor.matmul(acc[:, b, 0:3 * V], seed_w[:], mean_hl[:, e].rearrange("p t v -> p (t v)"),
                                         start=(e == 0), stop=False, skip_group_check=True)
                with pe.Fori(0, H) as h:
                    for s in range(RING):
                        u = (c * H + h) * RING + s
                        pe.wait_ge(words_ready, (u + 1) * Q4)
                        turn(u + 1, (s + 1) % RING)
                        for q in range(Q4):
                            pe.wait_ge(words_ready, (u + 1) * Q4 + q + 1)
                            tile = (h * RING + s) * Q4 + q
                            for t in range(CT):
                                for part, e in ((HI, 0), (HI, 1), (LO, 0)):
                                    last = nc.tensor.matmul(acc_of(t), words_h[:, q, t * P:(t + 1) * P, part],
                                                            val[:, bass.ds(tile, 1), e, 0:V].rearrange("p o v -> p (o v)"),
                                                            start=False, stop=False, skip_group_check=True)
                            last.then_inc(words_free, 1)


_INS = ['x', 'adj', 'L0_gnn_W', 'L0_gnn_a']
_OUTS = [((4096, 128), 'float32')]


def kernel(**inputs):
    import numpy as _np
    import concourse.bacc as _bacc
    from concourse import mybir as _mybir
    from concourse.bass_utils import run_bass_kernel_spmd as _run

    nc = _bacc.Bacc("TRN2", target_bir_lowering=False, num_devices=1)
    arrays, args = {}, []
    for name in _INS:
        a = _np.ascontiguousarray(inputs[name])
        arrays[f"in_{name}_dram"] = a
        args.append(nc.dram_tensor(f"in_{name}_dram", a.shape, _mybir.dt.from_np(a.dtype), kind="ExternalInput").ap())
    for i, (shape, dtype) in enumerate(_OUTS):
        dt = _mybir.dt.from_np(_np.dtype(dtype))
        args.append(nc.dram_tensor(f"out_{i}_dram", shape, dt, kind="ExternalOutput").ap())
    bass_graph_attention(nc, *args)
    r = _run(nc, [arrays], core_ids=[0])
    got = tuple(r.results[0][f"out_{i}_dram"] for i in range(len(_OUTS)))
    return got[0]
```

```python
from contextlib import ExitStack
import math

import concourse.bass as bass
from concourse import mybir

ALU = mybir.AluOpType
ACT = mybir.ActivationFunctionType
AX = mybir.AxisListType
F32 = mybir.dt.float32
F16 = mybir.dt.float16
BF16 = mybir.dt.bfloat16
I32 = mybir.dt.int32
U32 = mybir.dt.uint32
U8 = mybir.dt.uint8

P = 128
Q4 = 4
GROUP = Q4 * P
EPS = 1e-5
ALPHA = 0.2

B = 1.0 - ALPHA
LOG_WEIGHT = 7.5 * math.log(2.0)
LOG_VALUE = 10.0 * math.log(2.0)
SEED = 2.0 ** -60

RING = 4
DVE_HN, ACT_HN, POOL_HN = range(0, 4), range(4, 6), range(6, 8)
POOL_TILES = 2


def bass_graph_attention(nc: bass.Bass, x: bass.AP, adj: bass.AP, w: bass.AP, a: bass.AP, out: bass.AP):
    N, F = x.shape
    T = N // P
    G = N // GROUP
    CT = 8
    CHUNK = CT * P
    C = N // CHUNK
    H = G // RING
    STEPS = T // CT
    V = F + 1
    VP = V + 3
    BT = 3
    SLOTS = 3 * BT
    W2 = F + 2
    LO, HI = 0, 1
    assert F == P and w.shape == (F, F) and T % CT == 0 and G % RING == 0 and STEPS >= 2

    x_v = x.rearrange("(g p q) f -> p g q f", p=P, q=Q4)
    out_v = out.rearrange("(g p q) f -> g p q f", p=P, q=Q4)
    adj_v = adj.rearrange("(r p q) (g j) -> g r p q j", p=P, q=Q4, j=GROUP)

    with ExitStack() as ctx:
        def sb(name, shape, dt):
            return ctx.enter_context(nc.sbuf_tensor(name, shape, dt))

        def ps(name, shape, dt):
            return ctx.enter_context(nc.psum_tensor(name, shape, dt))

        def sem(name):
            return ctx.enter_context(nc.semaphore(name))

        x_sb = sb("x_sb", [P, T, F], F32)
        raw = sb("raw", [P, RING, CT, GROUP], I32)
        mask = sb("mask", [P, RING, CT, GROUP], U8)
        words = sb("words", [P, RING, CHUNK], F32)
        g_row = sb("g_row", [P, N], F32)
        val = sb("val", [P, T, 2, VP], F16)
        h_t = sb("h_t", [P, N], F32)
        hn = sb("hn", [P, 2, CT, F], F32)
        v32 = sb("v32", [P, 2, CT, F], F32)
        w_sb = sb("w_sb", [P, W2], F32)
        a_row = sb("a_row", [P, 2, F], F32)
        wa_prod = sb("wa_prod", [P, 2, F], F32)
        ident = sb("ident", [P, P], F32)
        ident_b = sb("ident_b", [P, P], BF16)
        seed_w = sb("seed_w", [P, P], BF16)
        log_weight = sb("log_weight", [P, 1], F32)
        log_value = sb("log_value", [P, 1], F32)
        step_bias = sb("step_bias", [P, 1], F32)
        minus_half = sb("minus_half", [P, CT], F32)
        stats = sb("stats", [P, T, 6], F32)
        mv = sb("mv", [P, T, 2], F32)
        var_eps = sb("var_eps", [P, T], F32)
        rstd = sb("rstd", [P, T], F32)
        nmr = sb("nmr", [P, T], F32)
        gq = sb("gq", [P, 2, STEPS * SLOTS], F32)
        gq_hi = sb("gq_hi", [P, 2, STEPS * SLOTS], F32)
        gq_word = sb("gq_word", [P, 2, STEPS * SLOTS], F32)
        dv = sb("dv", [P, STEPS * SLOTS], F32)
        h_sums = sb("h_sums", [P, 2 * STEPS], F32)
        h_sum = sb("h_sum", [P, 1], F32)
        mean32 = sb("mean32", [P, 3, V], F32)
        mean_hl = sb("mean_hl", [P, 2, 3, V], F16)
        acc_sb = sb("acc_sb", [P, 3, 3, V], F32)
        rz = sb("rz", [P, 3, 3], F32)
        hp = sb("hp", [P, CT, F], F32)
        neg = sb("neg", [P, CT, F], F32)
        pos = sb("pos", [P, CT, F], F32)

        acc = ps("acc", [P, 3, 512], F32)
        mask_t = ps("mask_t", [P, 2, 2, 512], F32)
        spread = ps("spread", [P, 512], F32)

        words_h = words[:].bitcast(F16).rearrange("p s (i e) -> p s i e", e=2)
        gq_word_h = gq_word[:].bitcast(F16).rearrange("p u (t e) -> p u t e", e=2)
        mask_pairs = mask[:].bitcast(BF16).rearrange("p s t (j h) -> p s t j h", h=2)
        maskt_pairs = mask_t[:].bitcast(BF16)
        maskt_bytes = mask_t[:].bitcast(U8).rearrange("p s h (i e) -> p s h i e", e=2)

        def acc_of(t):
            return acc[:, t // BT, (t % BT) * V:(t % BT + 1) * V]

        def projected(b, n):
            return acc[:, b, 0:n * W2].rearrange("p (t f) -> p t f", f=W2)

        def of_step(k, n=CT):
            return slice(k * SLOTS, k * SLOTS + n)

        x_in = [sem(f"x_in{k}") for k in range(STEPS)]
        w_in = sem("w_in")
        raw_in = [sem(f"raw_in{s}") for s in range(RING)]
        pool_bytes = sem("pool_bytes")
        act_bytes = sem("act_bytes")
        turned = sem("turned")
        words_ready = sem("words_ready")
        words_free = sem("words_free")
        acc_free = sem("acc_free")
        ident_ready = sem("ident_ready")
        consts = sem("consts")
        dve_chain = sem("dve_chain")
        var_ready = sem("var_ready")
        rstd_ready = sem("rstd_ready")
        nmr_ready = sem("nmr_ready")
        hn_dve = sem("hn_dve")
        hn_act = sem("hn_act")
        hn_pool = sem("hn_pool")
        wa_ready = sem("wa_ready")
        ht_ps = sem("ht_ps")
        ht_ready = sem("ht_ready")
        pad_ready = sem("pad_ready")
        wh_ps = sem("wh_ps")
        exps_ready = sem("exps_ready")
        word_ready = sem("word_ready")
        v32_ready = sem("v32_ready")
        vh_ready = sem("vh_ready")
        vl_ready = sem("vl_ready")
        z_ready = sem("z_ready")
        spread_ps = sem("spread_ps")
        grow_ready = sem("grow_ready")
        hsum_ready = sem("hsum_ready")
        mean_ps = sem("mean_ps")
        mean_ready = sem("mean_ready")
        rz_ready = sem("rz_ready")
        hp_ready = sem("hp_ready")
        neg_ready = sem("neg_ready")
        pos_ready = sem("pos_ready")
        ex_ready = sem("ex_ready")
        sum_ready = sem("sum_ready")
        res_ready = sem("res_ready")
        out_done = sem("out_done")

        block = ctx.enter_context(nc.Block())

        @block.sync
        def _(sp):
            for k in range(STEPS):
                sp.dma_start(x_sb[:, k * CT:(k + 1) * CT, :].rearrange("p (g q) f -> p g q f", q=Q4),
                             x_v[:, 2 * k:2 * k + 2]).then_inc(x_in[k], 16)
                if k == 0:
                    sp.dma_start(w_sb[:, 0:F], w).then_inc(w_in, 16)
                    sp.dma_start(a_row[:], a.rearrange("(k f) o -> o k f", k=2).broadcast_to([P, 2, F])).then_inc(w_in, 16)

            def load(c, g, s):
                for r in range(2):
                    sp.dma_start(raw[:, s, r * Q4:(r + 1) * Q4],
                                 adj_v[bass.ds(g, 1), bass.ds(c * 2 + r, 1)].rearrange("o r p q j -> (o r p) q j")
                                 ).then_inc(raw_in[s], 16)

            with sp.Fori(0, C) as c:
                with sp.Fori(0, H) as h:
                    for s in range(RING):
                        sp.wait_ge(pool_bytes, (c * H + h) * RING + s + 1)
                        sp.wait_ge(act_bytes, (c * H + h) * RING + s + 1)
                        load(c, h * RING + s, s)
            sp.wait_ge(out_done, 16 * 2 * C)

        @block.gpsimd
        def _(pool):
            nc.gpsimd.memset(ident[:], 0.0).then_inc(ident_ready, 1)
            pool.wait_ge(ident_ready, 1)
            nc.gpsimd.affine_select(out=ident[:], in_=ident[:], compare_op=ALU.not_equal, fill=1.0, base=0,
                                    pattern=[[-1, P]], channel_multiplier=1).then_inc(ident_ready, 1)
            pool.wait_ge(ident_ready, 2)
            nc.gpsimd.tensor_copy(ident_b[:], ident[:]).then_inc(ident_ready, 1)
            nc.gpsimd.memset(seed_w[:], SEED / P).then_inc(consts, 1)
            pool.sem_inc(pool_bytes, RING)
            pool.sem_inc(act_bytes, RING)
            pool.sem_inc(hp_ready, 1)
            def inverse_deviation(k):
                tt = slice(k * CT, (k + 1) * CT)
                pool.wait_ge(var_ready, k + 1)
                nc.gpsimd.tensor_tensor(rstd[:, tt], var_eps[:, tt], minus_half[:], ALU.pow).then_inc(rstd_ready, 1)
                pool.wait_ge(nmr_ready, k + 1)
                if k >= 2:
                    pool.wait_ge(ht_ps, 2 * k - 2)
                for i in POOL_HN:
                    t = k * CT + i
                    last = nc.gpsimd.tensor_scalar(hn[:, k % 2, i], x_sb[:, t], rstd[:, t:t + 1], nmr[:, t:t + 1], ALU.mult, ALU.add)
                last.then_inc(hn_pool, 1)

            def to_bytes(c, h, slots=range(RING)):
                for s in slots:
                    pool.wait_ge(raw_in[s], (c * H + h + 1) * 32)
                    pool.wait_ge(turned, (c * H + h) * RING + s + 1)
                    pool.nop(nofuse=True)
                    nc.gpsimd.tensor_scalar(mask[:, s, 0:POOL_TILES], raw[:, s, 0:POOL_TILES], 0, None,
                                            ALU.is_gt).then_inc(pool_bytes, 1)

            for k in range(STEPS):
                inverse_deviation(k)
            for k in range(STEPS):
                to_bytes(0, 0, range(k * RING // STEPS, (k + 1) * RING // STEPS))
                tt = slice(k * CT, (k + 1) * CT)
                pool.wait_ge(vh_ready, k + 1)
                nc.gpsimd.tensor_tensor(val[:, tt, 1, 0:F], v32[:, k % 2], val[:, tt, 0, 0:F], ALU.subtract).then_inc(vl_ready, 1)

            def tail(c):
                pool.wait_ge(rz_ready, c + 1)
                for b in range(3):
                    n = min(3, CT - 3 * b)
                    last = nc.gpsimd.tensor_tensor(hp[:, 3 * b:3 * b + n], acc_sb[:, b, 0:n, 0:F],
                                                   rz[:, b, 0:n].unsqueeze(2).broadcast_to([P, n, F]), ALU.mult)
                last.then_inc(hp_ready, 1)
                pool.wait_ge(hp_ready, c + 2)
                pool.nop(nofuse=True)
                nc.gpsimd.tensor_scalar(neg[:], hp[:], 0.0, None, ALU.min).then_inc(neg_ready, 1)
                pool.wait_ge(pos_ready, c + 1)
                nc.gpsimd.tensor_tensor(pos[:], pos[:], x_sb[:, bass.ds(c * CT, CT)], ALU.add).then_inc(sum_ready, 1)

            for h in range(1, H):
                to_bytes(0, h)
            with pool.Fori(1, C) as c:
                to_bytes(c, 0)
                tail(c - 1)
                for h in range(1, H):
                    to_bytes(c, h)
            pool.drain().then_inc(pool_bytes, 1)
            tail(C - 1)

        @block.scalar
        def _(act):
            act.sem_inc(acc_free, 3)
            act.wait_ge(consts, 4)
            def normalise(k):
                act.wait_ge(nmr_ready, k + 1)
                if k >= 2:
                    act.wait_ge(ht_ps, 2 * k - 2)
                for i in ACT_HN:
                    t = k * CT + i
                    last = nc.scalar.activation(hn[:, k % 2, i], x_sb[:, t], ACT.Identity, scale=rstd[:, t:t + 1], bias=nmr[:, t:t + 1])
                last.then_inc(hn_act, 1)

            def activations(k):
                for b in range(2):
                    c0 = k * CHUNK + b * GROUP
                    act.wait_ge(ht_ps, 2 * k + b + 1)
                    nc.scalar.activation(h_t[:, c0:c0 + GROUP], mask_t[:, k % 2, b, :], ACT.Relu,
                                         accum_out=h_sums[:, 2 * k + b:2 * k + b + 1]).then_inc(ht_ready, 1)

            def exponentials(k):
                act.wait_ge(wh_ps, 3 * k + 3)
                f1, f2 = (acc[:, :, 0:BT * W2].rearrange("p b (t f) -> p b t f", f=W2)[:, :, :, F + u] for u in range(2))
                ss = of_step(k, SLOTS)
                for row, f, scale, bias in ((dv[:, ss], f2, ALPHA, log_value), (gq[:, 0, ss], f1, -B, log_weight),
                                            (gq[:, 1, ss], f2, B, log_weight)):
                    nc.scalar.activation(row.rearrange("p (b t) -> p b t", t=BT), f, ACT.Exp, scale=scale,
                                         bias=bias[:, 0:1]).then_inc(exps_ready, 1)

            def spread_out(k, b):
                c0 = k * CHUNK + b * GROUP
                act.wait_ge(spread_ps, 2 * k + b + 1)
                nc.scalar.copy(g_row[:, c0:c0 + GROUP], spread[:]).then_inc(grow_ready, 1)

            def to_bytes(c, h, slots=range(RING)):
                for s in slots:
                    act.wait_ge(raw_in[s], (c * H + h + 1) * 32)
                    act.wait_ge(turned, (c * H + h) * RING + s + 1)
                    nc.scalar.activation(mask[:, s, POOL_TILES:CT], raw[:, s, POOL_TILES:CT], ACT.Sigmoid, scale=64.0,
                                         bias=step_bias[:, 0:1]).then_inc(act_bytes, 1)

            act.wait_ge(pad_ready, 1)
            normalise(0)
            normalise(1)
            activations(0)
            normalise(2)
            for k in range(STEPS):
                exponentials(k)
                if k == STEPS - 1:
                    to_bytes(0, 0, range(0, 1))
                if k >= 1:
                    spread_out(k - 1, 0)
                if k + 1 < STEPS:
                    activations(k + 1)
                if k >= 1:
                    spread_out(k - 1, 1)
                act.wait_ge(v32_ready, 3 * k + 3)
                nc.scalar.copy(val[:, k * CT:(k + 1) * CT, 0, 0:F], v32[:, k % 2]).then_inc(vh_ready, 1)
                if k + 3 < STEPS:
                    normalise(k + 3)
            to_bytes(0, 0, range(1, 2))
            spread_out(STEPS - 1, 0)
            spread_out(STEPS - 1, 1)
            to_bytes(0, 0, range(2, RING))

            def tail(c):
                act.wait_ge(words_free, RING + (c + 1) * G * Q4)
                act.wait_ge(hp_ready, c + 1)
                for b in range(3):
                    nc.scalar.copy(acc_sb[:, b], acc[:, b, 0:3 * V].rearrange("p (t v) -> p t v", v=V)).then_inc(acc_free, 1)
                act.wait_ge(hp_ready, c + 2)
                act.wait_ge(res_ready, c + 1)
                nc.scalar.activation(pos[:], hp[:], ACT.Relu).then_inc(pos_ready, 1)
                act.wait_ge(neg_ready, c + 1)
                nc.scalar.activation(neg[:], neg[:], ACT.Exp).then_inc(ex_ready, 1)

            def store(c):
                act.wait_ge(res_ready, c + 2)
                for r in range(2):
                    act.dma_start(out_v[bass.ds(2 * c + r, 1)].rearrange("o p q f -> (o p) q f"),
                                  x_sb[:, bass.ds(c * CT + r * Q4, Q4)]).then_inc(out_done, 16)

            for h in range(1, H):
                to_bytes(0, h)
            with act.Fori(1, C) as c:
                to_bytes(c, 0)
                tail(c - 1)
                for h in range(1, H):
                    to_bytes(c, h)
                store(c - 1)
            act.drain().then_inc(act_bytes, 1)
            tail(C - 1)
            store(C - 1)

        @block.vector
        def _(dve):
            links = [0]

            def link(ins):
                links[0] += 1
                ins.then_inc(dve_chain, 1)
                dve.wait_ge(dve_chain, links[0])

            dve.sem_inc(words_ready, Q4)
            nc.vector.memset(log_weight[:], LOG_WEIGHT).then_inc(consts, 1)
            nc.vector.memset(log_value[:], LOG_VALUE).then_inc(consts, 1)
            nc.vector.memset(step_bias[:], -32.0).then_inc(consts, 1)
            nc.vector.memset(acc[:, :, (BT - 1) * W2 + F:BT * W2], 0.0).then_inc(pad_ready, 1)
            link(nc.vector.memset(minus_half[:], -0.5))
            dve.sem_inc(res_ready, 1)

            def moments(k):
                dve.wait_ge(x_in[k], 16)
                for t in range(k * CT, (k + 1) * CT):
                    last = nc.vector.bn_stats(stats[:, t, :], x_sb[:, t, :])
                link(last)
                for t in range(k * CT, (k + 1) * CT):
                    last = nc.vector.bn_aggr(mv[:, t, :], stats[:, t, :])
                link(last)
                nc.vector.tensor_scalar(var_eps[:, k * CT:(k + 1) * CT], mv[:, k * CT:(k + 1) * CT, 1], EPS, None,
                                        ALU.add).then_inc(var_ready, 1)

            def normalise(k):
                dve.wait_ge(rstd_ready, k + 1)
                tt = slice(k * CT, (k + 1) * CT)
                nc.vector.scalar_tensor_tensor(nmr[:, tt], mv[:, tt, 0], -1.0, rstd[:, tt], ALU.mult, ALU.mult).then_inc(nmr_ready, 1)
                dve.wait_ge(nmr_ready, k + 1)
                if k >= 2:
                    dve.wait_ge(ht_ps, 2 * k - 2)
                for i in DVE_HN:
                    t = k * CT + i
                    last = nc.vector.tensor_scalar(hn[:, k % 2, i], x_sb[:, t], rstd[:, t:t + 1], nmr[:, t:t + 1], ALU.mult, ALU.add)
                last.then_inc(hn_dve, 1)

            def make_words(k):
                tt, ss = slice(k * CT, (k + 1) * CT), of_step(k)
                dve.wait_ge(exps_ready, 3 * k + 3)
                link(nc.vector.tensor_scalar(gq_hi[:, :, ss].bitcast(U32), gq[:, :, ss].bitcast(U32), 0xFFFFE000, None,
                                             ALU.bitwise_and))
                nc.vector.tensor_copy(gq_word_h[:, :, ss, HI], gq_hi[:, :, ss]).then_inc(word_ready, 1)
                nc.vector.tensor_tensor(gq_word_h[:, :, ss, LO], gq[:, :, ss], gq_hi[:, :, ss], ALU.subtract).then_inc(word_ready, 1)
                link(nc.vector.tensor_copy(val[:, tt, 0, F], dv[:, ss]))
                nc.vector.tensor_tensor(val[:, tt, 1, F], dv[:, ss], val[:, tt, 0, F], ALU.subtract).then_inc(z_ready, 1)

            def weigh(k):
                dve.wait_ge(exps_ready, 3 * k + 3)
                if k >= 2:
                    dve.wait_ge(vl_ready, k - 1)
                for b in range(3):
                    n = min(BT, CT - b * BT)
                    i0 = k * SLOTS + b * BT
                    nc.vector.tensor_tensor(v32[:, k % 2, b * BT:b * BT + n], projected(b, n)[:, :, 0:F],
                                            dv[:, i0:i0 + n].unsqueeze(2).broadcast_to([P, n, F]), ALU.mult
                                            ).then_inc(v32_ready, 1)

            moments(0)
            moments(1)
            normalise(0)
            dve.wait_ge(w_in, 32)
            link(nc.vector.tensor_tensor(wa_prod[:], a_row[:], w_sb[:, 0:F].unsqueeze(1).broadcast_to([P, 2, F]), ALU.mult))
            nc.vector.tensor_reduce(w_sb[:, F:W2], wa_prod[:], AX.X, ALU.add).then_inc(wa_ready, 1)
            for k in range(2, STEPS):
                moments(k)
                normalise(k - 1)
            normalise(STEPS - 1)
            nc.vector.memset(mean32[:], 2.0 ** 10)
            for k in range(STEPS):
                weigh(k)
                make_words(k)
                if k == STEPS - 2:
                    dve.wait_ge(ht_ready, 2 * STEPS)
                    nc.vector.tensor_reduce(h_sum[:], h_sums[:], AX.X, ALU.add).then_inc(hsum_ready, 1)
            dve.wait_ge(mean_ps, 1)
            link(nc.vector.tensor_scalar(mean32[:, :, 0:F], mask_t[:, 1, 0, 0:F].unsqueeze(1).broadcast_to([P, 3, F]), 2.0 ** 10 / N,
                                         None, ALU.mult))
            link(nc.vector.tensor_copy(mean_hl[:, 0], mean32[:]))
            nc.vector.tensor_tensor(mean_hl[:, 1], mean32[:], mean_hl[:, 0], ALU.subtract).then_inc(mean_ready, 1)

            dve.wait_ge(grow_ready, 2)

            def slot_of(h, s, q):
                per_step = CT // Q4
                return (h * (RING // per_step) + s // per_step) * SLOTS + s % per_step * Q4 + q

            def weights(c, h, s):
                for q in range(Q4):
                    u = (c * H + h) * RING + s
                    if q == 0:
                        dve.wait_ge(turned, RING + u + 1)
                    dve.wait_ge(words_free, u * Q4 + q + 1)
                    nc.vector.scalar_tensor_tensor(words[:, q, :], g_row[:, bass.ds(c * CHUNK, CHUNK)],
                                                   gq_word[:, 1, bass.ds(slot_of(h, s, q), 1)],
                                                   maskt_bytes[:, s % 2, q // 2, :, q % 2], ALU.max, ALU.mult).then_inc(words_ready, 1)

            def reciprocals(c):
                dve.wait_ge(acc_free, 3 * (c + 2))
                nc.vector.reciprocal(rz[:], acc_sb[:, :, :, F]).then_inc(rz_ready, 1)

            def result(c):
                dve.wait_ge(ex_ready, c + 1)
                dve.wait_ge(sum_ready, c + 1)
                nc.vector.scalar_tensor_tensor(x_sb[:, bass.ds(c * CT, CT)], neg[:], -1.0, pos[:], ALU.add, ALU.add).then_inc(res_ready, 1)

            with dve.Fori(0, H) as h:
                for s in range(RING):
                    weights(0, h, s)
            dve.wait_ge(grow_ready, 2 * STEPS)
            with dve.Fori(1, C) as c:
                weights(c, 0, 0)
                reciprocals(c - 1)
                for s in range(1, RING):
                    weights(c, 0, s)
                result(c - 1)
                for h in range(1, H):
                    for s in range(RING):
                        weights(c, h, s)
            reciprocals(C - 1)
            result(C - 1)

        @block.tensor
        def _(pe):
            pe.sem_inc(turned, RING)
            pe.sem_inc(words_free, RING)
            pe.wait_ge(ident_ready, 3)

            def turn_x(k):
                pe.wait_ge(hn_dve, k + 1)
                pe.wait_ge(hn_act, k + 1)
                pe.wait_ge(hn_pool, k + 1)
                if k >= 2:
                    pe.wait_ge(ht_ready, 2 * k - 2)
                for i in range(CT):
                    ins = nc.tensor.transpose(mask_t[:, k % 2, i // Q4, (i % Q4) * P:(i % Q4 + 1) * P], hn[:, k % 2, i], ident[:])
                    if i % Q4 == Q4 - 1:
                        ins.then_inc(ht_ps, 1)

            def project(k):
                pe.wait_ge(ht_ready, 2 * k + 2)
                if k >= 1:
                    pe.wait_ge(exps_ready, 3 * k)
                for i in range(CT):
                    t, b = k * CT + i, i // BT
                    if i % BT == 0 and k >= 1:
                        pe.wait_ge(v32_ready, 3 * k - 2 + b)
                    ins = nc.tensor.matmul(projected(b, BT)[:, i % BT], h_t[:, t * P:(t + 1) * P], w_sb[:], start=True, stop=True)
                    if i % BT == BT - 1 or i == CT - 1:
                        ins.then_inc(wh_ps, 1)

            def spread_words(k, b):
                pe.wait_ge(word_ready, 2 * k + 2)
                if 2 * k + b >= 1:
                    pe.wait_ge(grow_ready, 2 * k + b)
                for q in range(Q4):
                    i = k * SLOTS + b * Q4 + q
                    last = nc.tensor.transpose(spread[:, q * P:(q + 1) * P], gq_word[:, 0, i:i + 1].broadcast_to([P, P]), ident[:])
                last.then_inc(spread_ps, 1)

            turn_x(0)
            turn_x(1)
            pe.wait_ge(wa_ready, 1)
            pe.wait_ge(pad_ready, 1)
            for k in range(STEPS):
                project(k)
                if k >= 1:
                    spread_words(k - 1, 0)
                if k + 2 < STEPS:
                    turn_x(k + 2)
                if k >= 1:
                    spread_words(k - 1, 1)
            pe.wait_ge(hsum_ready, 1)
            nc.tensor.matmul(mask_t[:, 1, 0, 0:F], h_sum[:, 0:1].broadcast_to([P, P]), w_sb[:, 0:F], start=True, stop=True).then_inc(mean_ps, 1)

            def turn(u, s):
                pe.wait_ge(pool_bytes, RING + u + 1)
                pe.wait_ge(act_bytes, RING + u + 1)
                for half in range(2):
                    for i in range(CT):
                        last = nc.tensor.transpose(maskt_pairs[:, s % 2, half, i * P:(i + 1) * P], mask_pairs[:, s, i, :, half],
                                                   ident_b[:])
                last.then_inc(turned, 1)

            pe.wait_ge(ht_ready, 2 * STEPS)
            turn(0, 0)
            spread_words(STEPS - 1, 0)
            spread_words(STEPS - 1, 1)
            pe.wait_ge(mean_ready, 1)
            pe.wait_ge(v32_ready, 3 * STEPS)
            pe.wait_ge(z_ready, STEPS)
            with pe.Fori(0, C) as c:
                for b in range(3):
                    pe.wait_ge(acc_free, 3 * c + b + 1)
                    for e in range(2):
                        nc.tensor.matmul(acc[:, b, 0:3 * V], seed_w[:], mean_hl[:, e].rearrange("p t v -> p (t v)"),
                                         start=(e == 0), stop=False, skip_group_check=True)
                with pe.Fori(0, H) as h:
                    for s in range(RING):
                        u = (c * H + h) * RING + s
                        pe.wait_ge(words_ready, (u + 1) * Q4)
                        turn(u + 1, (s + 1) % RING)
                        pe.wait_ge(vl_ready, h * (STEPS // H) + s * STEPS // H // RING + 1)
                        for q in range(Q4):
                            pe.wait_ge(words_ready, (u + 1) * Q4 + q + 1)
                            tile = (h * RING + s) * Q4 + q
                            for t in range(CT):
                                for part, e in ((HI, 0), (HI, 1), (LO, 0)):
                                    last = nc.tensor.matmul(acc_of(t), words_h[:, q, t * P:(t + 1) * P, part],
                                                            val[:, bass.ds(tile, 1), e, 0:V].rearrange("p o v -> p (o v)"),
                                                            start=False, stop=False, skip_group_check=True)
                            last.then_inc(words_free, 1)


_INS = ['x', 'adj', 'L0_gnn_W', 'L0_gnn_a']
_OUTS = [((4096, 128), 'float32')]


def kernel(**inputs):
    import numpy as _np
    import concourse.bacc as _bacc
    from concourse import mybir as _mybir
    from concourse.bass_utils import run_bass_kernel_spmd as _run

    nc = _bacc.Bacc("TRN2", target_bir_lowering=False, num_devices=1)
    arrays, args = {}, []
    for name in _INS:
        a = _np.ascontiguousarray(inputs[name])
        arrays[f"in_{name}_dram"] = a
        args.append(nc.dram_tensor(f"in_{name}_dram", a.shape, _mybir.dt.from_np(a.dtype), kind="ExternalInput").ap())
    for i, (shape, dtype) in enumerate(_OUTS):
        dt = _mybir.dt.from_np(_np.dtype(dtype))
        args.append(nc.dram_tensor(f"out_{i}_dram", shape, dt, kind="ExternalOutput").ap())
    bass_graph_attention(nc, *args)
    r = _run(nc, [arrays], core_ids=[0])
    got = tuple(r.results[0][f"out_{i}_dram"] for i in range(len(_OUTS)))
    return got[0]
```

```python
from contextlib import ExitStack
import math

import concourse.bass as bass
from concourse import mybir

ALU = mybir.AluOpType
ACT = mybir.ActivationFunctionType
AX = mybir.AxisListType
F32 = mybir.dt.float32
F16 = mybir.dt.float16
BF16 = mybir.dt.bfloat16
I32 = mybir.dt.int32
U32 = mybir.dt.uint32
U8 = mybir.dt.uint8

P = 128
GT = 8
GROUP = GT * P
CT = 4
CHUNK = CT * P
EPS = 1e-5
ALPHA = 0.2

B = 1.0 - ALPHA
LOG_WEIGHT = 7.5 * math.log(2.0)
LOG_VALUE = 10.0 * math.log(2.0)
SEED = 2.0 ** -60

WEIGHT_RANGE = (0.6, 60000.0)
VALUE_SQUARES = 60000.0 ** 2
VALUE_RMS = 4.0
MASKED = 9e15

RING = 4
HALF = 4
DVE_HN, ACT_HN, POOL_HN = range(0, 4), range(4, 6), range(6, 8)
POOL_TILES = 1
FIRST_POOL_TILES = (2, 2, 1, 1)


def bass_graph_attention(nc: bass.Bass, x: bass.AP, adj: bass.AP, w: bass.AP, a: bass.AP, out: bass.AP):
    N, F = x.shape
    T = N // P
    G = N // GROUP
    C = N // CHUNK
    V = F + 1
    BT = 3
    SLOTS = 3 * BT
    W2 = F + 2
    LO, HI = 0, 1
    assert F == P and w.shape == (F, F) and G == RING and GT == 2 * CT == 2 * HALF

    x_v = x.rearrange("(g p q) f -> g p q f", p=P, q=GT)
    out_v = out.rearrange("(r p k q) f -> r k p q f", p=P, k=2, q=CT)
    adj_v = adj.rearrange("(r p k q) (g j) -> g r k p q j", p=P, k=2, q=CT, j=GROUP)

    adj_rows_v = adj.rearrange("(g p q) j -> g p q j", p=P, q=GT)
    out_rows_v = out.rearrange("(g p q) f -> g p q f", p=P, q=GT)

    with ExitStack() as ctx:
        def sb(name, shape, dt):
            return ctx.enter_context(nc.sbuf_tensor(name, shape, dt))

        def ps(name, shape, dt):
            return ctx.enter_context(nc.psum_tensor(name, shape, dt))

        def sem(name):
            return ctx.enter_context(nc.semaphore(name))

        x_sb = sb("x_sb", [P, T, F], F32)
        raw = sb("raw", [P, RING, CT, GROUP], I32)
        mask = sb("mask", [P, RING, CT, GROUP], U8)
        words = sb("words", [P, 2, HALF, CHUNK], F32)
        g_row = sb("g_row", [P, N], F32)
        val = sb("val", [P, T, 2, V], F16)
        h_t = sb("h_t", [P, N], F32)
        hn = sb("hn", [P, 2, GT, F], F32)
        v32 = sb("v32", [P, 2, GT, F], F32)
        w_sb = sb("w_sb", [P, W2], F32)
        a_row = sb("a_row", [P, 2, F], F32)
        wa_prod = sb("wa_prod", [P, 2, F], F32)
        ident = sb("ident", [P, P], F32)
        ident_b = sb("ident_b", [P, P], BF16)
        seed_w = sb("seed_w", [P, P], BF16)
        log_weight = sb("log_weight", [P, 1], F32)
        log_value = sb("log_value", [P, 1], F32)
        step_bias = sb("step_bias", [P, 1], F32)
        minus_half = sb("minus_half", [P, GT], F32)
        stats = sb("stats", [P, T, 6], F32)
        mv = sb("mv", [P, T, 2], F32)
        var_eps = sb("var_eps", [P, T], F32)
        rstd = sb("rstd", [P, T], F32)
        nmr = sb("nmr", [P, T], F32)
        gq = sb("gq", [P, 2, G * SLOTS], F32)
        gq_hi = sb("gq_hi", [P, 2, G * SLOTS], F32)
        gq_word = sb("gq_word", [P, 2, G * SLOTS], F32)
        dv = sb("dv", [P, G * SLOTS], F32)
        h_sums = sb("h_sums", [P, 2 * G], F32)
        h_sum = sb("h_sum", [P, 1], F32)
        mean32 = sb("mean32", [P, V], F32)
        mean_hl = sb("mean_hl", [P, 2, V], F16)
        acc_sb = sb("acc_sb", [P, CT, 2, V], F32)
        num = sb("num", [P, CT, V], F32)
        rz = sb("rz", [P, CT], F32)
        hp = sb("hp", [P, CT, F], F32)
        neg = sb("neg", [P, CT, F], F32)
        pos = sb("pos", [P, CT, F], F32)

        ones = sb("ones", [P, 1], F32)
        squares = sb("squares", [P, G], F32)
        in_range = sb("in_range", [P, 2 * G * SLOTS + G], F32)
        above_low = sb("above_low", [P, 2 * G * SLOTS], F32)
        check = sb("check", [P, 2], F32)
        outside = sb("outside", [1, 2], F32)
        general = sb("general", [1, 1], I32)

        slot = [raw[:, s].rearrange("p t j -> p (t j)") for s in range(RING)]
        wh = slot[0].bitcast(F32).rearrange("p (t f) -> p t f", f=F)
        adj_rows = slot[1]
        score = slot[2].bitcast(F32)
        keep = slot[3].bitcast(F32)
        weights_t = keep.rearrange("p (t i) -> p t i", i=P)
        f2_row = g_row[:]
        f12 = sb("f12", [P, 2, T], F32)
        row_max = sb("row_max", [P, 2], F32)
        row_sum = sb("row_sum", [P, 2], F32)
        x_tile, res_tile, hp_tile, pos_tile, neg_tile = hn[:, 0, 0], hn[:, 0, 1], hn[:, 0, 2], hn[:, 0, 3], hn[:, 0, 4]

        acc = ps("acc", [P, CT, 512], F32)
        mask_t = ps("mask_t", [P, 2, 2, 512], F32)

        words_h = words[:].bitcast(F16).rearrange("p s q (i e) -> p s q i e", e=2)
        gq_word_h = gq_word[:].bitcast(F16).rearrange("p u (t e) -> p u t e", e=2)
        mask_pairs = mask[:].bitcast(BF16).rearrange("p s t (j h) -> p s t j h", h=HALF)
        maskt_pairs = mask_t[:].bitcast(BF16).rearrange("p s b (h i) -> p s (b h) i", h=2)
        maskt_bytes = mask_t[:].bitcast(U8).rearrange("p s b (h i e) -> p s (b h) i e", h=2, e=2)
        spread = acc[:, 3, :]

        def wait_tile_done(engine, c, t):
            if t < CT - 1:
                engine.wait_ge(acc_done, (CT - 1) * c + t + 1)
            else:
                engine.wait_ge(words_free, 2 + 2 * RING * (c + 1))

        def projected(b, n):
            return acc[:, b, 0:n * W2].rearrange("p (t f) -> p t f", f=W2)

        def of_step(k, n=GT):
            return slice(k * SLOTS, k * SLOTS + n)

        x_in = [sem(f"x_in{k}") for k in range(G)]
        w_in = sem("w_in")
        raw_in = [sem(f"raw_in{s}") for s in range(RING)]
        pool_bytes = sem("pool_bytes")
        act_bytes = sem("act_bytes")
        turned = sem("turned")
        words_ready = sem("words_ready")
        words_free = sem("words_free")
        acc_done = sem("acc_done")
        acc_free = sem("acc_free")
        ident_ready = sem("ident_ready")
        consts = sem("consts")
        dve_chain = sem("dve_chain")
        var_ready = sem("var_ready")
        rstd_ready = sem("rstd_ready")
        nmr_ready = sem("nmr_ready")
        hn_dve = sem("hn_dve")
        hn_act = sem("hn_act")
        hn_pool = sem("hn_pool")
        wa_ready = sem("wa_ready")
        ht_ps = sem("ht_ps")
        ht_ready = sem("ht_ready")
        pad_ready = sem("pad_ready")
        wh_ps = sem("wh_ps")
        exps_ready = sem("exps_ready")
        word_ready = sem("word_ready")
        v32_ready = sem("v32_ready")
        vh_ready = sem("vh_ready")
        vl_ready = sem("vl_ready")
        z_ready = sem("z_ready")
        spread_ps = sem("spread_ps")
        grow_ready = sem("grow_ready")
        hsum_ready = sem("hsum_ready")
        mean_ps = sem("mean_ps")
        mean_ready = sem("mean_ready")
        num_ready = sem("num_ready")
        rz_ready = sem("rz_ready")
        hp_ready = sem("hp_ready")
        neg_ready = sem("neg_ready")
        pos_ready = sem("pos_ready")
        ex_ready = sem("ex_ready")
        sum_ready = sem("sum_ready")
        res_ready = sem("res_ready")
        last_neg = sem("last_neg")
        last_pos = sem("last_pos")
        last_low = sem("last_low")
        last_sum = sem("last_sum")
        last_ex = sem("last_ex")
        last_res = sem("last_res")
        out_done = sem("out_done")
        squares_ready = sem("squares_ready")
        check_ready = sem("check_ready")
        check_ps = sem("check_ps")
        general_ready = sem("general_ready")
        gen_proj = sem("gen_proj")
        gen_wh = sem("gen_wh")
        gen_spread = sem("gen_spread")
        gen_row = sem("gen_row")
        gen_in = sem("gen_in")
        gen_step = sem("gen_step")
        gen_max = sem("gen_max")
        gen_exp = sem("gen_exp")
        gen_turned = sem("gen_turned")
        gen_copied = sem("gen_copied")
        gen_prod = sem("gen_prod")
        gen_neg = sem("gen_neg")
        gen_elu = sem("gen_elu")
        gen_res = sem("gen_res")
        gen_out = sem("gen_out")
        GEN_STEPS = 10

        block = ctx.enter_context(nc.Block())

        @block.sync
        def _(sp):
            for k in range(G):
                sp.dma_start(x_sb[:, k * GT:(k + 1) * GT, :], x_v[k]).then_inc(x_in[k], 16)
                if k == 0:
                    sp.dma_start(w_sb[:, 0:F], w).then_inc(w_in, 16)
                    sp.dma_start(a_row[:], a.rearrange("(k f) o -> o k f", k=2).broadcast_to([P, 2, F])).then_inc(w_in, 16)

            with sp.Fori(0, C // 2) as r:
                with sp.Fori(0, 2) as k:
                    for s in range(RING):
                        sp.wait_ge(pool_bytes, (2 * r + k) * RING + s + 1)
                        sp.wait_ge(act_bytes, (2 * r + k) * RING + s + 1)
                        sp.dma_start(raw[:, s], adj_v[s, bass.ds(r, 1), bass.ds(k, 1)].rearrange("r k p q j -> (r k p) q j")
                                     ).then_inc(raw_in[s], 16)
            sp.wait_ge(general_ready, 1)
            with sp.If(sp.value_load(general[0:1, 0:1], min_val=0, max_val=1) > 0):
                sp.wait_ge(out_done, 16 * C)
                with sp.Fori(0, G) as g:
                    with sp.Fori(0, GT) as q:
                        sp.wait_ge(gen_res, g * GT + q + 1)
                        sp.nop(nofuse=True)
                        sp.dma_start(adj_rows, adj_rows_v[bass.ds(g, 1), :, bass.ds(q, 1)].rearrange("g p q j -> (g p q) j")
                                     ).then_inc(gen_in, 16)
                        sp.dma_start(x_tile, x_v[bass.ds(g, 1), :, bass.ds(q, 1)].rearrange("g p q f -> (g p q) f")
                                     ).then_inc(gen_in, 16)
                        sp.wait_ge(gen_res, g * GT + q + 2)
                        sp.nop(nofuse=True)
                        sp.dma_start(out_rows_v[bass.ds(g, 1), :, bass.ds(q, 1)].rearrange("g p q f -> (g p q) f"), res_tile
                                     ).then_inc(gen_out, 16)
                        sp.wait_ge(gen_out, (g * GT + q + 1) * 16)
                        sp.nop(nofuse=True)
            sp.wait_ge(out_done, 16 * C)

        @block.gpsimd
        def _(pool):
            nc.gpsimd.memset(ident[:], 0.0).then_inc(ident_ready, 1)
            pool.wait_ge(ident_ready, 1)
            nc.gpsimd.affine_select(out=ident[:], in_=ident[:], compare_op=ALU.not_equal, fill=1.0, base=0,
                                    pattern=[[-1, P]], channel_multiplier=1).then_inc(ident_ready, 1)
            pool.wait_ge(ident_ready, 2)
            nc.gpsimd.tensor_copy(ident_b[:], ident[:]).then_inc(ident_ready, 1)
            nc.gpsimd.memset(ones[:], 1.0)
            nc.gpsimd.memset(seed_w[:], SEED / P).then_inc(consts, 1)
            pool.sem_inc(pool_bytes, RING)
            pool.sem_inc(act_bytes, RING)
            pool.sem_inc(hp_ready, 1)
            def inverse_deviation(k):
                tt = slice(k * GT, (k + 1) * GT)
                pool.wait_ge(var_ready, k + 1)
                nc.gpsimd.tensor_tensor(rstd[:, tt], var_eps[:, tt], minus_half[:], ALU.pow).then_inc(rstd_ready, 1)
                pool.wait_ge(nmr_ready, k + 1)
                if k >= 2:
                    pool.wait_ge(ht_ps, 2 * k - 2)
                for i in POOL_HN:
                    t = k * GT + i
                    last = nc.gpsimd.tensor_scalar(hn[:, k % 2, i], x_sb[:, t], rstd[:, t:t + 1], nmr[:, t:t + 1], ALU.mult, ALU.add)
                last.then_inc(hn_pool, 1)

            def to_bytes(c, slots=range(RING), tiles=(POOL_TILES,) * RING):
                for s in slots:
                    pool.wait_ge(raw_in[s], (c + 1) * 16)
                    pool.wait_ge(turned, c * RING + s + 1)
                    pool.nop(nofuse=True)
                    nc.gpsimd.tensor_scalar(mask[:, s, 0:tiles[s]], raw[:, s, 0:tiles[s]], 0, None,
                                            ALU.is_gt).then_inc(pool_bytes, 1)

            for k in range(G):
                inverse_deviation(k)
            for k in range(G):
                to_bytes(0, range(k * RING // G, (k + 1) * RING // G), FIRST_POOL_TILES)
                tt = slice(k * GT, (k + 1) * GT)
                pool.wait_ge(vh_ready, k + 1)
                nc.gpsimd.tensor_tensor(val[:, tt, 1, 0:F], v32[:, k % 2], val[:, tt, 0, 0:F], ALU.subtract).then_inc(vl_ready, 1)

            def tail(c):
                pool.wait_ge(acc_free, CT * (c + 2))
                nc.gpsimd.tensor_tensor(num[:], acc_sb[:, :, 0], acc_sb[:, :, 1], ALU.add).then_inc(num_ready, 1)
                pool.wait_ge(rz_ready, c + 1)
                nc.gpsimd.tensor_tensor(hp[:], num[:, :, 0:F], rz[:].unsqueeze(2).broadcast_to([P, CT, F]), ALU.mult
                                        ).then_inc(hp_ready, 1)
                pool.wait_ge(hp_ready, c + 2)
                pool.nop(nofuse=True)
                nc.gpsimd.tensor_scalar(neg[:], hp[:], 0.0, None, ALU.min).then_inc(neg_ready, 1)
                pool.wait_ge(pos_ready, c + 1)
                nc.gpsimd.tensor_tensor(pos[:], pos[:], x_sb[:, bass.ds(c * CT, CT)], ALU.add).then_inc(sum_ready, 1)

            with pool.Fori(1, C) as c:
                to_bytes(c)
                tail(c - 1)
            pool.drain().then_inc(pool_bytes, 1)
            for t in range(CT):
                pool.wait_ge(last_pos, t + 1)
                nc.gpsimd.tensor_tensor(hp[:, t], pos[:, t], x_sb[:, (C - 1) * CT + t], ALU.add).then_inc(last_sum, 1)

        @block.scalar
        def _(act):
            act.sem_inc(acc_free, CT)
            act.wait_ge(consts, 4)
            def normalise(k):
                act.wait_ge(nmr_ready, k + 1)
                if k >= 2:
                    act.wait_ge(ht_ps, 2 * k - 2)
                for i in ACT_HN:
                    t = k * GT + i
                    last = nc.scalar.activation(hn[:, k % 2, i], x_sb[:, t], ACT.Identity, scale=rstd[:, t:t + 1], bias=nmr[:, t:t + 1])
                last.then_inc(hn_act, 1)

            def activations(k):
                for b in range(2):
                    c0 = k * GROUP + b * 512
                    act.wait_ge(ht_ps, 2 * k + b + 1)
                    nc.scalar.activation(h_t[:, c0:c0 + 512], mask_t[:, k % 2, b, :], ACT.Relu,
                                         accum_out=h_sums[:, 2 * k + b:2 * k + b + 1]).then_inc(ht_ready, 1)

            def exponentials(k):
                act.wait_ge(wh_ps, 3 * k + 3)
                f1, f2 = (acc[:, 0:3, 0:BT * W2].rearrange("p b (t f) -> p b t f", f=W2)[:, :, :, F + u] for u in range(2))
                ss = of_step(k, SLOTS)
                for row, f, scale, bias in ((dv[:, ss], f2, ALPHA, log_value), (gq[:, 0, ss], f1, -B, log_weight),
                                            (gq[:, 1, ss], f2, B, log_weight)):
                    nc.scalar.activation(row.rearrange("p (b t) -> p b t", t=BT), f, ACT.Exp, scale=scale,
                                         bias=bias[:, 0:1]).then_inc(exps_ready, 1)

            def spread_out(k, b):
                c0 = k * GROUP + b * 512
                act.wait_ge(spread_ps, 2 * k + b + 1)
                nc.scalar.copy(g_row[:, c0:c0 + 512], spread).then_inc(grow_ready, 1)

            def to_bytes(c, slots=range(RING), tiles=(POOL_TILES,) * RING):
                for s in slots:
                    act.wait_ge(raw_in[s], (c + 1) * 16)
                    act.wait_ge(turned, c * RING + s + 1)
                    nc.scalar.activation(mask[:, s, tiles[s]:CT], raw[:, s, tiles[s]:CT], ACT.Sigmoid, scale=64.0,
                                         bias=step_bias[:, 0:1]).then_inc(act_bytes, 1)

            act.wait_ge(pad_ready, 1)
            normalise(0)
            normalise(1)
            activations(0)
            normalise(2)
            for k in range(G):
                exponentials(k)
                if k >= 1:
                    spread_out(k - 1, 0)
                if k + 1 < G:
                    activations(k + 1)
                if k >= 1:
                    spread_out(k - 1, 1)
                if k == G - 1:
                    to_bytes(0, range(0, 1), FIRST_POOL_TILES)
                act.wait_ge(v32_ready, 3 * k + 3)
                nc.scalar.copy(val[:, k * GT:(k + 1) * GT, 0, 0:F], v32[:, k % 2]).then_inc(vh_ready, 1)
                if k + 3 < G:
                    normalise(k + 3)
            spread_out(G - 1, 0)
            spread_out(G - 1, 1)
            to_bytes(0, range(1, RING), FIRST_POOL_TILES)

            act.wait_ge(vh_ready, G)
            for k in range(G):
                nc.scalar.activation(acc_sb[:].rearrange("p t e v -> p (t e v)")[:, 0:GT * F].rearrange("p (t f) -> p t f", f=F),
                                     val[:, k * GT:(k + 1) * GT, 0, 0:F], ACT.Square,
                                     accum_out=squares[:, k:k + 1]).then_inc(squares_ready, 1)
                act.wait_ge(squares_ready, k + 1)

            def tail(c):
                act.wait_ge(hp_ready, c + 1)
                for t in range(CT):
                    wait_tile_done(act, c, t)
                    nc.scalar.copy(acc_sb[:, t], acc[:, t, 0:2 * V].rearrange("p (e v) -> p e v", v=V)).then_inc(acc_free, 1)
                act.wait_ge(hp_ready, c + 2)
                act.wait_ge(res_ready, c + 1)
                nc.scalar.activation(pos[:], hp[:], ACT.Relu).then_inc(pos_ready, 1)
                act.wait_ge(neg_ready, c + 1)
                nc.scalar.activation(neg[:], neg[:], ACT.Exp).then_inc(ex_ready, 1)

            def store(c):
                act.wait_ge(res_ready, c + 2)
                act.dma_start(out_v[bass.ds(c // 2, 1), bass.ds(c % 2, 1)].rearrange("r k p q f -> (r k p) q f"),
                              x_sb[:, bass.ds(c * CT, CT)]).then_inc(out_done, 16)

            with act.Fori(1, C) as c:
                to_bytes(c)
                tail(c - 1)
                store(c - 1)
            act.drain().then_inc(act_bytes, 1)
            def last_exponential(t):
                act.wait_ge(last_neg, t + 1)
                nc.scalar.activation(neg[:, t], neg[:, t], ACT.Exp).then_inc(last_ex, 1)

            act.wait_ge(hp_ready, C)
            for t in range(CT):
                wait_tile_done(act, C - 1, t)
                nc.scalar.copy(acc_sb[:, t, 1], acc[:, t, V:2 * V]).then_inc(last_low, 1)
                if t >= 1:
                    last_exponential(t - 1)
            last_exponential(CT - 1)
            act.wait_ge(last_res, CT)
            act.dma_start(out_v[C // 2 - 1, 1], x_sb[:, (C - 1) * CT:C * CT]).then_inc(out_done, 16)

            act.wait_ge(general_ready, 1)
            with act.If(act.value_load(general[0:1, 0:1], min_val=0, max_val=1) > 0):
                act.sem_inc(gen_row, 1)
                with act.Fori(0, T) as t:
                    act.wait_ge(gen_spread, t + 1)
                    nc.scalar.copy(f2_row[:, bass.ds(t * P, P)], acc[:, 1, 0:P]).then_inc(gen_row, 1)
                with act.Fori(0, T) as t:
                    act.wait_ge(gen_max, t + 1)
                    nc.scalar.activation(score, score, ACT.Exp, bias=row_max[:, 1:2], accum_out=row_sum[:, 0:1]
                                         ).then_inc(gen_exp, 1)
                    act.wait_ge(gen_neg, t + 1)
                    nc.scalar.activation(neg_tile, neg_tile, ACT.Exp).then_inc(gen_elu, 1)

        @block.vector
        def _(dve):
            links = [0]

            def link(ins):
                links[0] += 1
                ins.then_inc(dve_chain, 1)
                dve.wait_ge(dve_chain, links[0])

            dve.sem_inc(words_ready, HALF)
            nc.vector.memset(log_weight[:], LOG_WEIGHT).then_inc(consts, 1)
            nc.vector.memset(log_value[:], LOG_VALUE).then_inc(consts, 1)
            nc.vector.memset(step_bias[:], -32.0).then_inc(consts, 1)
            nc.vector.memset(acc[:, 0:3, (BT - 1) * W2 + F:BT * W2], 0.0).then_inc(pad_ready, 1)
            link(nc.vector.memset(minus_half[:], -0.5))
            dve.sem_inc(res_ready, 1)

            def moments(k):
                dve.wait_ge(x_in[k], 16)
                for t in range(k * GT, (k + 1) * GT):
                    last = nc.vector.bn_stats(stats[:, t, :], x_sb[:, t, :])
                link(last)
                for t in range(k * GT, (k + 1) * GT):
                    last = nc.vector.bn_aggr(mv[:, t, :], stats[:, t, :])
                link(last)
                nc.vector.tensor_scalar(var_eps[:, k * GT:(k + 1) * GT], mv[:, k * GT:(k + 1) * GT, 1], EPS, None,
                                        ALU.add).then_inc(var_ready, 1)

            def normalise(k):
                dve.wait_ge(rstd_ready, k + 1)
                tt = slice(k * GT, (k + 1) * GT)
                nc.vector.scalar_tensor_tensor(nmr[:, tt], mv[:, tt, 0], -1.0, rstd[:, tt], ALU.mult, ALU.mult).then_inc(nmr_ready, 1)
                dve.wait_ge(nmr_ready, k + 1)
                if k >= 2:
                    dve.wait_ge(ht_ps, 2 * k - 2)
                for i in DVE_HN:
                    t = k * GT + i
                    last = nc.vector.tensor_scalar(hn[:, k % 2, i], x_sb[:, t], rstd[:, t:t + 1], nmr[:, t:t + 1], ALU.mult, ALU.add)
                last.then_inc(hn_dve, 1)

            def make_words(k):
                tt, ss = slice(k * GT, (k + 1) * GT), of_step(k)
                dve.wait_ge(exps_ready, 3 * k + 3)
                link(nc.vector.tensor_scalar(gq_hi[:, :, ss].bitcast(U32), gq[:, :, ss].bitcast(U32), 0xFFFFE000, None,
                                             ALU.bitwise_and))
                nc.vector.tensor_copy(gq_word_h[:, :, ss, HI], gq_hi[:, :, ss]).then_inc(word_ready, 1)
                nc.vector.tensor_tensor(gq_word_h[:, :, ss, LO], gq[:, :, ss], gq_hi[:, :, ss], ALU.subtract).then_inc(word_ready, 1)
                link(nc.vector.tensor_copy(val[:, tt, 0, F], dv[:, ss]))
                nc.vector.tensor_tensor(val[:, tt, 1, F], dv[:, ss], val[:, tt, 0, F], ALU.subtract).then_inc(z_ready, 1)

            def weigh(k):
                dve.wait_ge(exps_ready, 3 * k + 3)
                if k >= 2:
                    dve.wait_ge(vl_ready, k - 1)
                for b in range(3):
                    n = min(BT, GT - b * BT)
                    i0 = k * SLOTS + b * BT
                    nc.vector.tensor_tensor(v32[:, k % 2, b * BT:b * BT + n], projected(b, n)[:, :, 0:F],
                                            dv[:, i0:i0 + n].unsqueeze(2).broadcast_to([P, n, F]), ALU.mult
                                            ).then_inc(v32_ready, 1)

            moments(0)
            moments(1)
            normalise(0)
            dve.wait_ge(w_in, 32)
            link(nc.vector.tensor_tensor(wa_prod[:], a_row[:], w_sb[:, 0:F].unsqueeze(1).broadcast_to([P, 2, F]), ALU.mult))
            nc.vector.tensor_reduce(w_sb[:, F:W2], wa_prod[:], AX.X, ALU.add).then_inc(wa_ready, 1)
            for k in range(2, G):
                moments(k)
                normalise(k - 1)
            normalise(G - 1)
            nc.vector.memset(mean32[:], 2.0 ** 10)
            for k in range(G):
                weigh(k)
                make_words(k)
                if k == G - 2:
                    dve.wait_ge(ht_ready, 2 * G)
                    nc.vector.tensor_reduce(h_sum[:], h_sums[:], AX.X, ALU.add).then_inc(hsum_ready, 1)
            dve.wait_ge(mean_ps, 1)
            link(nc.vector.tensor_scalar(mean32[:, 0:F], mask_t[:, 1, 0, 0:F], 2.0 ** 10 / N, None, ALU.mult))
            link(nc.vector.tensor_copy(mean_hl[:, 0], mean32[:]))
            nc.vector.tensor_tensor(mean_hl[:, 1], mean32[:], mean_hl[:, 0], ALU.subtract).then_inc(mean_ready, 1)

            dve.wait_ge(grow_ready, 2)

            def weights(c, s, qs=range(GT)):
                for q in qs:
                    if q == 0:
                        dve.wait_ge(turned, c * RING + s + RING + 1)
                    if q % HALF == 0:
                        dve.wait_ge(words_free, (c * RING + s) * 2 + q // HALF + 1)
                    k = s * SLOTS + q
                    nc.vector.scalar_tensor_tensor(words[:, q // HALF, q % HALF, :], g_row[:, bass.ds(c * CHUNK, CHUNK)],
                                                   gq_word[:, 1, k:k + 1], maskt_bytes[:, s % 2, q // 2, :, q % 2],
                                                   ALU.max, ALU.mult).then_inc(words_ready, 1)

            def reciprocals(c):
                dve.wait_ge(num_ready, c + 1)
                nc.vector.reciprocal(rz[:], num[:, :, F]).then_inc(rz_ready, 1)

            def result(c):
                dve.wait_ge(ex_ready, c + 1)
                dve.wait_ge(sum_ready, c + 1)
                nc.vector.scalar_tensor_tensor(x_sb[:, bass.ds(c * CT, CT)], neg[:], -1.0, pos[:], ALU.add, ALU.add
                                               ).then_inc(res_ready, 1)

            for s in range(RING):
                weights(0, s)
            dve.wait_ge(grow_ready, 2 * G)
            with dve.Fori(1, C) as c:
                weights(c, 0, range(HALF + 2))
                reciprocals(c - 1)
                weights(c, 0, range(HALF + 2, GT))
                weights(c, 1)
                result(c - 1)
                weights(c, 2)
                for s in range(3, RING):
                    weights(c, s)

            def last_result(t):
                tile = (C - 1) * CT + t
                dve.wait_ge(last_sum, t + 1)
                dve.wait_ge(last_ex, t + 1)
                nc.vector.scalar_tensor_tensor(x_sb[:, tile], neg[:, t], -1.0, hp[:, t], ALU.add, ALU.add).then_inc(
                    last_res, 1)

            dve.wait_ge(squares_ready, G)
            W = 2 * G * SLOTS
            gq_all = gq[:].rearrange("p u t -> p (u t)")
            link(nc.vector.tensor_scalar(above_low[:], gq_all, WEIGHT_RANGE[0], None, ALU.is_ge))
            nc.vector.scalar_tensor_tensor(in_range[:, 0:W], gq_all, WEIGHT_RANGE[1], above_low[:], ALU.is_le, ALU.mult)
            link(nc.vector.tensor_scalar(in_range[:, W:W + G], squares[:], VALUE_SQUARES, None, ALU.is_le))
            nc.vector.tensor_reduce(check[:, 0:1], in_range[:], AX.X, ALU.add)
            nc.vector.tensor_reduce(check[:, 1:2], squares[:], AX.X, ALU.add).then_inc(check_ready, 1)

            dve.wait_ge(hp_ready, C)
            for t in range(CT):
                dve.wait_ge(last_low, t + 1)
                link(nc.vector.tensor_tensor(num[:, t], acc[:, t, 0:V], acc_sb[:, t, 1], ALU.add))
                link(nc.vector.reciprocal(rz[:, t:t + 1], num[:, t, F:V]))
                nc.vector.tensor_scalar(neg[:, t], num[:, t, 0:F], rz[:, t:t + 1], 0.0, ALU.mult, ALU.min).then_inc(last_neg, 1)
                nc.vector.tensor_scalar(pos[:, t], num[:, t, 0:F], rz[:, t:t + 1], 0.0, ALU.mult, ALU.max).then_inc(last_pos, 1)
                if t >= 1:
                    last_result(t - 1)
            last_result(CT - 1)

            dve.wait_ge(check_ps, 1)
            nc.vector.tensor_scalar(outside[:, 0:1], mask_t[0:1, 1, 0, 0:1], P * (W + G) - 0.5, None, ALU.is_lt)
            link(nc.vector.tensor_scalar(outside[:, 1:2], mask_t[0:1, 1, 0, 1:2], N * F * VALUE_RMS ** 2, None, ALU.is_lt))
            link(nc.vector.tensor_tensor(general[:], outside[:, 0:1], outside[:, 1:2], ALU.max))
            dve.wait_ge(pool_bytes, RING * (C + 1) + 1)
            dve.wait_ge(act_bytes, RING * (C + 1) + 1)
            dve.drain().then_inc(general_ready, 1)
            with dve.If(dve.value_load(general[0:1, 0:1], min_val=0, max_val=1) > 0):
                dve.sem_inc(gen_wh, 1)
                dve.sem_inc(gen_copied, 1)
                dve.sem_inc(gen_res, 1)
                with dve.Fori(0, T) as t:
                    dve.wait_ge(gen_proj, t + 1)
                    nc.vector.tensor_copy(wh[:, bass.ds(t, 1)], acc[:, 0:1, 0:F])
                    nc.vector.tensor_copy(f12[:, :, bass.ds(t, 1)], acc[:, 0, F:W2].unsqueeze(2)).then_inc(gen_wh, 1)
                dve.wait_ge(gen_row, T + 1)
                with dve.Fori(0, T) as t:
                    step = [0]

                    def then(ins):
                        step[0] += 1
                        ins.then_inc(gen_step, 1)
                        dve.wait_ge(gen_step, t * GEN_STEPS + step[0])

                    dve.wait_ge(gen_in, (t + 1) * 32)
                    nc.vector.tensor_scalar(keep.rearrange("p (g q j) -> p g q j", g=G, q=GT),
                                            adj_rows.rearrange("p (g j q) -> p g q j", g=G, q=GT), 0, None, ALU.is_gt)
                    then(nc.vector.tensor_scalar(score, f2_row, f12[:, 0, bass.ds(t, 1)], None, ALU.add))
                    then(nc.vector.scalar_tensor_tensor(score, score, ALPHA, score, ALU.mult, ALU.max))
                    then(nc.vector.tensor_tensor(score, score, keep, ALU.mult))
                    then(nc.vector.tensor_scalar(keep, keep, MASKED, -MASKED, ALU.mult, ALU.add))
                    then(nc.vector.tensor_tensor(score, score, keep, ALU.add))
                    then(nc.vector.tensor_reduce(row_max[:, 0:1], score, AX.X, ALU.max))
                    nc.vector.tensor_scalar(row_max[:, 1:2], row_max[:, 0:1], -1.0, None, ALU.mult).then_inc(gen_max, 1)
                    for half in range(2):
                        dve.wait_ge(gen_turned, 2 * t + half + 1)
                        nc.vector.tensor_copy(keep[:, half * N // 2:(half + 1) * N // 2].rearrange("p (b j) -> p b j", j=512),
                                              acc[:]).then_inc(gen_copied, 1)
                    dve.wait_ge(gen_exp, t + 1)
                    then(nc.vector.reciprocal(row_sum[:, 1:2], row_sum[:, 0:1]))
                    dve.wait_ge(gen_prod, t + 1)
                    then(nc.vector.tensor_scalar(hp_tile, mask_t[:, 1, 1, 0:F], row_sum[:, 1:2], None, ALU.mult))
                    nc.vector.tensor_scalar(neg_tile, hp_tile, 0.0, None, ALU.min).then_inc(gen_neg, 1)
                    then(nc.vector.tensor_scalar(pos_tile, hp_tile, 0.0, None, ALU.max))
                    then(nc.vector.tensor_tensor(pos_tile, pos_tile, x_tile, ALU.add))
                    dve.wait_ge(gen_elu, t + 1)
                    assert step[0] == GEN_STEPS
                    nc.vector.scalar_tensor_tensor(res_tile, neg_tile, -1.0, pos_tile, ALU.add, ALU.add).then_inc(gen_res, 1)

        @block.tensor
        def _(pe):
            pe.sem_inc(turned, RING)
            pe.sem_inc(words_free, 2)
            pe.wait_ge(ident_ready, 3)

            def turn_x(k):
                pe.wait_ge(hn_dve, k + 1)
                pe.wait_ge(hn_act, k + 1)
                pe.wait_ge(hn_pool, k + 1)
                if k >= 2:
                    pe.wait_ge(ht_ready, 2 * k - 2)
                for i in range(GT):
                    ins = nc.tensor.transpose(mask_t[:, k % 2, i // 4, (i % 4) * P:(i % 4 + 1) * P], hn[:, k % 2, i], ident[:])
                    if i % 4 == 3:
                        ins.then_inc(ht_ps, 1)

            def project(k):
                pe.wait_ge(ht_ready, 2 * k + 2)
                if k >= 1:
                    pe.wait_ge(exps_ready, 3 * k)
                for i in range(GT):
                    t, b = k * GT + i, i // BT
                    if i % BT == 0 and k >= 1:
                        pe.wait_ge(v32_ready, 3 * k - 2 + b)
                    ins = nc.tensor.matmul(projected(b, BT)[:, i % BT], h_t[:, t * P:(t + 1) * P], w_sb[:], start=True, stop=True)
                    if i % BT == BT - 1 or i == GT - 1:
                        ins.then_inc(wh_ps, 1)

            def spread_words(k, b):
                pe.wait_ge(word_ready, 2 * k + 2)
                if 2 * k + b >= 1:
                    pe.wait_ge(grow_ready, 2 * k + b)
                for q in range(4):
                    i = k * SLOTS + 4 * b + q
                    last = nc.tensor.transpose(spread[:, q * P:(q + 1) * P], gq_word[:, 0, i:i + 1].broadcast_to([P, P]), ident[:])
                last.then_inc(spread_ps, 1)

            turn_x(0)
            turn_x(1)
            pe.wait_ge(wa_ready, 1)
            pe.wait_ge(pad_ready, 1)
            for k in range(G):
                project(k)
                if k >= 1:
                    spread_words(k - 1, 0)
                if k + 2 < G:
                    turn_x(k + 2)
                if k >= 1:
                    spread_words(k - 1, 1)
            pe.wait_ge(hsum_ready, 1)
            nc.tensor.matmul(mask_t[:, 1, 0, 0:F], h_sum[:, 0:1].broadcast_to([P, P]), w_sb[:, 0:F], start=True, stop=True).then_inc(mean_ps, 1)

            def turn(u, s):
                pe.wait_ge(pool_bytes, RING + u + 1)
                pe.wait_ge(act_bytes, RING + u + 1)
                for h in range(HALF):
                    for i in range(CT):
                        last = nc.tensor.transpose(maskt_pairs[:, s % 2, h, i * P:(i + 1) * P], mask_pairs[:, s, i, :, h], ident_b[:])
                last.then_inc(turned, 1)

            pe.wait_ge(ht_ready, 2 * G)
            turn(0, 0)
            spread_words(G - 1, 0)
            spread_words(G - 1, 1)
            pe.wait_ge(mean_ready, 1)
            pe.wait_ge(v32_ready, 3 * G)
            pe.wait_ge(grow_ready, 2 * G)
            pe.wait_ge(z_ready, G)
            with pe.Fori(0, C) as c:
                for s in range(RING):
                    u = c * RING + s
                    pe.wait_ge(words_ready, u * GT + HALF)
                    turn(u + 1, (s + 1) % RING)
                    pe.wait_ge(vl_ready, s + 1)
                    for half in range(2):
                        pe.wait_ge(words_ready, u * GT + half * HALF + 2 * HALF)
                        for t in range(CT):
                            if s == 0 and half == 0:
                                pe.wait_ge(acc_free, CT * c + t + 1)
                                nc.tensor.matmul(acc[:, t, 0:2 * V], seed_w[:], mean_hl[:].rearrange("p e v -> p (e v)"),
                                                 start=True, stop=False, skip_group_check=True)
                            for q in range(HALF):
                                tile = s * GT + half * HALF + q
                                high = words_h[:, half, q, t * P:(t + 1) * P, HI]
                                low = words_h[:, half, q, t * P:(t + 1) * P, LO]
                                nc.tensor.matmul(acc[:, t, 0:2 * V], high, val[:, tile].rearrange("p e v -> p (e v)"),
                                                 start=False, stop=False, skip_group_check=True)
                                last = nc.tensor.matmul(acc[:, t, 0:V], low, val[:, tile, 0],
                                                        start=False, stop=False, skip_group_check=True)
                            if s == RING - 1 and half == 1 and t < CT - 1:
                                last.then_inc(acc_done, 1)
                        last.then_inc(words_free, 1)

            pe.wait_ge(check_ready, 1)
            pe.wait_ge(words_ready, C * RING * GT + HALF)
            nc.tensor.matmul(mask_t[0:1, 1, 0, 0:2], ones[:], check[:], start=True, stop=True).then_inc(check_ps, 1)

            pe.wait_ge(general_ready, 1)
            with pe.If(pe.value_load(general[0:1, 0:1], min_val=0, max_val=1) > 0):
                for t in range(T):
                    pe.wait_ge(gen_wh, t + 1)
                    nc.tensor.matmul(acc[:, 0, 0:W2], h_t[:, t * P:(t + 1) * P], w_sb[:], start=True, stop=True).then_inc(gen_proj, 1)
                    pe.wait_ge(gen_wh, t + 2)
                    pe.wait_ge(gen_row, t + 1)
                    nc.tensor.transpose(acc[:, 1, 0:P], f12[:, 1, t:t + 1].broadcast_to([P, P]), ident[:]).then_inc(gen_spread, 1)
                pe.wait_ge(gen_row, T + 1)
                with pe.Fori(0, T) as t:
                    pe.wait_ge(gen_exp, t + 1)
                    for half in range(2):
                        pe.wait_ge(gen_copied, 2 * t + half + 1)
                        for i in range(T // 2):
                            j = half * T // 2 + i
                            last = nc.tensor.transpose(acc[:, i // 4, (i % 4) * P:(i % 4 + 1) * P], score[:, j * P:(j + 1) * P], ident[:])
                        last.then_inc(gen_turned, 1)
                    pe.wait_ge(gen_copied, 2 * t + 3)
                    pe.wait_ge(gen_res, t + 1)
                    for j in range(T):
                        last = nc.tensor.matmul(mask_t[:, 1, 1, 0:F], weights_t[:, j], wh[:, j], start=(j == 0), stop=(j == T - 1))
                    last.then_inc(gen_prod, 1)


_INS = ['x', 'adj', 'L0_gnn_W', 'L0_gnn_a']
_OUTS = [((4096, 128), 'float32')]


def kernel(**inputs):
    import numpy as _np
    import concourse.bacc as _bacc
    from concourse import mybir as _mybir
    from concourse.bass_utils import run_bass_kernel_spmd as _run

    nc = _bacc.Bacc("TRN2", target_bir_lowering=False, num_devices=1)
    arrays, args = {}, []
    for name in _INS:
        a = _np.ascontiguousarray(inputs[name])
        arrays[f"in_{name}_dram"] = a
        args.append(nc.dram_tensor(f"in_{name}_dram", a.shape, _mybir.dt.from_np(a.dtype), kind="ExternalInput").ap())
    for i, (shape, dtype) in enumerate(_OUTS):
        dt = _mybir.dt.from_np(_np.dtype(dtype))
        args.append(nc.dram_tensor(f"out_{i}_dram", shape, dt, kind="ExternalOutput").ap())
    bass_graph_attention(nc, *args)
    r = _run(nc, [arrays], core_ids=[0])
    got = tuple(r.results[0][f"out_{i}_dram"] for i in range(len(_OUTS)))
    return got[0]
```
